# Optimizing a Trainium2 kernel written in Bass

```python
import numpy as np
import jax
import jax.numpy as jnp

def _softmax(x, axis=-1):
    return jax.nn.softmax(x, axis=axis)

def _gelu(x):
    return jax.nn.gelu(x, approximate=True)

def _silu(x):
    return jax.nn.silu(x)

def _sigmoid(x):
    return jax.nn.sigmoid(x)

def _layernorm(x, axis=-1, eps=1e-05):
    m = jnp.mean(x, axis=axis, keepdims=True)
    v = jnp.var(x, axis=axis, keepdims=True)
    return (x - m) / jnp.sqrt(v + eps)

def _scatter_add(tgt, idx, src, axis=0):
    return tgt.at[idx].add(src)

def _segment_sum(src, seg, n):
    return jax.ops.segment_sum(src, seg, n)
kernel_name = 'mk_rec_standalone_d1_rec_r8_924779'

def setup_inputs(seed: int=0):
    np.random.seed(seed)
    _w = jnp.asarray

    def _rec_inputs():
        import jax
        import jax.numpy as jnp
        _rk = jax.random.key(seed)
        r_last_memory = -0.00340659 + 1.00146 * jax.random.normal(jax.random.fold_in(_rk, 1), (512, 512), jnp.float32)
        r_all_memory = -2.88516e-05 + 0.999852 * jax.random.normal(jax.random.fold_in(_rk, 2), (512, 200, 512), jnp.float32)
        r_mask = jnp.stack([jax.random.randint(jax.random.fold_in(jax.random.fold_in(_rk, 3), 0), (512,), 773, 99578, jnp.int32), jax.random.randint(jax.random.fold_in(jax.random.fold_in(_rk, 3), 1), (512,), 1445, 99969, jnp.int32), jax.random.randint(jax.random.fold_in(jax.random.fold_in(_rk, 3), 2), (512,), 109, 12464, jnp.int32), jax.random.randint(jax.random.fold_in(jax.random.fold_in(_rk, 3), 3), (512,), 175, 98555, jnp.int32), jax.random.randint(jax.random.fold_in(jax.random.fold_in(_rk, 3), 4), (512,), 187, 98951, jnp.int32), jax.random.randint(jax.random.fold_in(jax.random.fold_in(_rk, 3), 5), (512,), 1331, 99662, jnp.int32), jax.random.randint(jax.random.fold_in(jax.random.fold_in(_rk, 3), 6), (512,), 132, 99964, jnp.int32), jax.random.randint(jax.random.fold_in(jax.random.fold_in(_rk, 3), 7), (512,), 335, 98055, jnp.int32), jax.random.randint(jax.random.fold_in(jax.random.fold_in(_rk, 3), 8), (512,), 616, 99887, jnp.int32), jax.random.randint(jax.random.fold_in(jax.random.fold_in(_rk, 3), 9), (512,), 655, 99694, jnp.int32), jax.random.randint(jax.random.fold_in(jax.random.fold_in(_rk, 3), 10), (512,), 577, 98148, jnp.int32), jax.random.randint(jax.random.fold_in(jax.random.fold_in(_rk, 3), 11), (512,), 32, 99257, jnp.int32), jax.random.randint(jax.random.fold_in(jax.random.fold_in(_rk, 3), 12), (512,), 466, 12455, jnp.int32), jax.random.randint(jax.random.fold_in(jax.random.fold_in(_rk, 3), 13), (512,), 229, 99539, jnp.int32), jax.random.randint(jax.random.fold_in(jax.random.fold_in(_rk, 3), 14), (512,), 148, 99685, jnp.int32), jax.random.randint(jax.random.fold_in(jax.random.fold_in(_rk, 3), 15), (512,), 131, 99938, jnp.int32), jax.random.randint(jax.random.fold_in(jax.random.fold_in(_rk, 3), 16), (512,), 517, 99723, jnp.int32), jax.random.randint(jax.random.fold_in(jax.random.fold_in(_rk, 3), 17), (512,), 61, 99469, jnp.int32), jax.random.randint(jax.random.fold_in(jax.random.fold_in(_rk, 3), 18), (512,), 103, 99481, jnp.int32), jax.random.randint(jax.random.fold_in(jax.random.fold_in(_rk, 3), 19), (512,), 662, 99614, jnp.int32), jax.random.randint(jax.random.fold_in(jax.random.fold_in(_rk, 3), 20), (512,), 1126, 98957, jnp.int32), jax.random.randint(jax.random.fold_in(jax.random.fold_in(_rk, 3), 21), (512,), 15, 99995, jnp.int32), jax.random.randint(jax.random.fold_in(jax.random.fold_in(_rk, 3), 22), (512,), 198, 99434, jnp.int32), jax.random.randint(jax.random.fold_in(jax.random.fold_in(_rk, 3), 23), (512,), 93, 99657, jnp.int32), jax.random.randint(jax.random.fold_in(jax.random.fold_in(_rk, 3), 24), (512,), 196, 99580, jnp.int32), jax.random.randint(jax.random.fold_in(jax.random.fold_in(_rk, 3), 25), (512,), 92, 99871, jnp.int32), jax.random.randint(jax.random.fold_in(jax.random.fold_in(_rk, 3), 26), (512,), 296, 99193, jnp.int32), jax.random.randint(jax.random.fold_in(jax.random.fold_in(_rk, 3), 27), (512,), 243, 99588, jnp.int32), jax.random.randint(jax.random.fold_in(jax.random.fold_in(_rk, 3), 28), (512,), 200, 99531, jnp.int32), jax.random.randint(jax.random.fold_in(jax.random.fold_in(_rk, 3), 29), (512,), 674, 99708, jnp.int32), jax.random.randint(jax.random.fold_in(jax.random.fold_in(_rk, 3), 30), (512,), 518, 99974, jnp.int32), jax.random.randint(jax.random.fold_in(jax.random.fold_in(_rk, 3), 31), (512,), 52, 99762, jnp.int32), jax.random.randint(jax.random.fold_in(jax.random.fold_in(_rk, 3), 32), (512,), 599, 99927, jnp.int32), jax.random.randint(jax.random.fold_in(jax.random.fold_in(_rk, 3), 33), (512,), 1313, 99941, jnp.int32), jax.random.randint(jax.random.fold_in(jax.random.fold_in(_rk, 3), 34), (512,), 120, 99927, jnp.int32), jax.random.randint(jax.random.fold_in(jax.random.fold_in(_rk, 3), 35), (512,), 424, 98705, jnp.int32), jax.random.randint(jax.random.fold_in(jax.random.fold_in(_rk, 3), 36), (512,), 784, 99431, jnp.int32), jax.random.randint(jax.random.fold_in(jax.random.fold_in(_rk, 3), 37), (512,), 597, 99722, jnp.int32), jax.random.randint(jax.random.fold_in(jax.random.fold_in(_rk, 3), 38), (512,), 336, 99753, jnp.int32), jax.random.randint(jax.random.fold_in(jax.random.fold_in(_rk, 3), 39), (512,), 200, 12457, jnp.int32), jax.random.randint(jax.random.fold_in(jax.random.fold_in(_rk, 3), 40), (512,), 120, 98767, jnp.int32), jax.random.randint(jax.random.fold_in(jax.random.fold_in(_rk, 3), 41), (512,), 165, 99917, jnp.int32), jax.random.randint(jax.random.fold_in(jax.random.fold_in(_rk, 3), 42), (512,), 814, 99905, jnp.int32), jax.random.randint(jax.random.fold_in(jax.random.fold_in(_rk, 3), 43), (512,), 647, 98581, jnp.int32), jax.random.randint(jax.random.fold_in(jax.random.fold_in(_rk, 3), 44), (512,), 2393, 99390, jnp.int32), jax.random.randint(jax.random.fold_in(jax.random.fold_in(_rk, 3), 45), (512,), 296, 99767, jnp.int32), jax.random.randint(jax.random.fold_in(jax.random.fold_in(_rk, 3), 46), (512,), 399, 12416, jnp.int32), jax.random.randint(jax.random.fold_in(jax.random.fold_in(_rk, 3), 47), (512,), 303, 12466, jnp.int32), jax.random.randint(jax.random.fold_in(jax.random.fold_in(_rk, 3), 48), (512,), 680, 99463, jnp.int32), jax.random.randint(jax.random.fold_in(jax.random.fold_in(_rk, 3), 49), (512,), 53, 99444, jnp.int32)], axis=1)
        return (r_last_memory, r_all_memory, r_mask)
    r_last_memory, r_all_memory, r_mask = _rec_inputs()

    def _L0_rec_setup():
        import jax, jax.numpy as jnp
        import numpy as np
        B, S, H = (256, 200, 512)
        ITEMS, HIST = (12500, 50)
        key = jax.random.key(seed)
        ks = jax.random.split(key, 7)
        return {'last_memory': jax.random.normal(ks[0], (B, H), dtype=jnp.float32), 'all_memory': jax.random.normal(ks[1], (B, S, H), dtype=jnp.float32), 'item_matrix_transpose': jax.random.normal(ks[2], (2 * H, ITEMS), dtype=jnp.float32) * 0.02, 'mask': jax.random.randint(ks[3], (B, HIST), 0, ITEMS), 'We': jax.random.normal(ks[4], (H, H), dtype=jnp.float32) * (1.0 / np.sqrt(H)), 'Ue': jax.random.normal(ks[5], (H, H), dtype=jnp.float32) * (1.0 / np.sqrt(H)), 'Ve': jax.random.normal(ks[6], (1, H), dtype=jnp.float32) * (1.0 / np.sqrt(H))}
    _L0_rec_all = _L0_rec_setup()
    _L0_rec_in = {k: v for k, v in _L0_rec_all.items() if k in ('item_matrix_transpose', 'We', 'Ue', 'Ve')}
    del _L0_rec_all
    return {'r_last_memory': r_last_memory, 'r_all_memory': r_all_memory, 'r_mask': r_mask, 'L0_rec_item_matrix_transpose': _L0_rec_in['item_matrix_transpose'], 'L0_rec_We': _L0_rec_in['We'], 'L0_rec_Ue': _L0_rec_in['Ue'], 'L0_rec_Ve': _L0_rec_in['Ve']}

def reference(r_last_memory, r_all_memory, r_mask, L0_rec_item_matrix_transpose, L0_rec_We, L0_rec_Ue, L0_rec_Ve):
    import jax
    import jax.numpy as jnp

    def _L0_rec_ref(last_memory, all_memory, item_matrix_transpose, mask, We, Ue, Ve):
        import jax, jax.numpy as jnp
        import numpy as np
        B, S, H = (256, 200, 512)
        ITEMS, HIST = (12500, 50)
        q = last_memory @ We.T
        k = jnp.einsum('bsh,ih->bsi', all_memory, Ue)
        score = jnp.einsum('bsh,h->bs', jnp.tanh(q[:, None, :] + k), Ve[0])
        attn = jax.nn.softmax(score, axis=1)
        ctx = jnp.einsum('bs,bsh->bh', attn, all_memory)
        cat = jnp.concatenate([ctx, last_memory], axis=1)
        logits = cat @ item_matrix_transpose
        rows = jnp.arange(logits.shape[0])[:, None]
        logits = logits.at[rows, mask].set(-1000000000.0)
        return jax.nn.softmax(logits, axis=1)
    y = _L0_rec_ref(r_last_memory, r_all_memory, L0_rec_item_matrix_transpose, r_mask, L0_rec_We, L0_rec_Ue, L0_rec_Ve)
    return y

_drawn_inputs = setup_inputs


def setup_inputs(seed=0):
    import zlib

    import numpy as np

    out = dict(_drawn_inputs(seed))
    spreads = {}
    factors = {'L0_rec_We': 43.613, 'L0_rec_Ue': 5.794, 'L0_rec_Ve': 5.915}
    for name, (base, spread) in spreads.items():
        noise = np.random.default_rng([zlib.crc32(name.encode()), seed]).standard_normal(out[name].shape)
        drawn = base * np.exp(spread * noise) if base else spread * noise
        out[name] = jnp.asarray(drawn.astype(out[name].dtype))
    for name, factor in factors.items():
        out[name] = (out[name] * factor).astype(out[name].dtype)
    return out
```

```python
from contextlib import ExitStack

import numpy as np
import concourse.bass as bass
from concourse import mybir

ALU = mybir.AluOpType
ACT = mybir.ActivationFunctionType
AX_X = mybir.AxisListType.X
F32 = mybir.dt.float32
F32R = mybir.dt.float32r
BF16 = mybir.dt.bfloat16
I32 = mybir.dt.int32
U32 = mybir.dt.uint32

P = 128
MASKED = -1000000000.0
STEP_ROWS = 2
SLOTS = 4
CHUNK = 500
PIECE = 2
GROUP = 5


def wait(eng, sem, count):
    if not isinstance(count, int) or count > 0:
        eng.wait_ge(sem, count)


def attention_rank(nc, x_l, last_l, we_l, ue_l, ve_l, items_l, hist, out):
    STEPS, _, KT, COLS = x_l.shape
    S = COLS // STEP_ROWS
    B = last_l.shape[2]
    H = KT * P
    BODIES = STEPS // SLOTS
    BODY_ROWS = SLOTS * STEP_ROWS
    CHUNKS, PIECES = items_l.shape[0:2]
    ITEMS = CHUNKS * CHUNK
    HIST = hist.shape[1]
    ROW_TILES = B // P
    HALVES = 2
    RT = ROW_TILES // HALVES
    HALF = RT * P
    GROUPS = CHUNKS // GROUP
    CT = PIECES * PIECE
    COLUMNS = ROW_TILES * HIST
    SCATTER_BODIES = COLUMNS // SLOTS
    assert B == STEPS * STEP_ROWS == BODIES * BODY_ROWS and CHUNKS == GROUPS * GROUP
    assert CT == 2 * KT and SCATTER_BODIES * SLOTS == COLUMNS and SCATTER_BODIES < BODIES

    mask_bias = nc.dram_tensor("mask_bias", (B * ITEMS, 1), BF16, kind="Internal").ap()
    mask_rows = mask_bias.rearrange("(b i) o -> b (i o)", b=B)

    with ExitStack() as ctx:
        def sb(name, shape, dt):
            return ctx.enter_context(nc.sbuf_tensor(name, shape, dt))

        def sem(name):
            return ctx.enter_context(nc.semaphore(name))

        def shared(name, shape, dt):
            start = -(-nc.sbuf_base // 32) * 32
            tensor = sb(name, shape, dt)
            taken = [start]

            def under(name, shape, dt):
                at = taken[0]
                taken[0] = at + 4 * int(np.prod(shape[1:]))
                assert taken[0] <= start + 4 * int(np.prod(tensor.shape[1:]))
                return nc.alloc_sbuf_tensor_at(name, shape, dt, offset=at)
            return tensor, under

        we_at = -(-nc.sbuf_base // 32) * 32
        probs, under_probs = shared("probs", [P, RT, ITEMS], F32)
        th = [under_probs(f"th{s}", [P, KT, COLS], F32) for s in range(2)]
        we_raw = nc.alloc_sbuf_tensor_at("we_raw", [P, KT, H], F32, offset=we_at)

        x = [under_probs(f"x{s}", [P, KT, COLS], F32) for s in range(SLOTS)]
        x_hi = [under_probs(f"x_hi{s}", [P, KT, COLS], F32R) for s in range(2)]
        x_lo = [under_probs(f"x_lo{s}", [P, KT, COLS], F32R) for s in range(2)]
        ue_hi = under_probs("ue_hi", [P, KT, H], F32R)
        ue_lo = under_probs("ue_lo", [P, KT, H], F32R)
        q_t = under_probs("q_t", [P, KT, B], F32)
        weighted = under_probs("weighted", [P, 2, COLS], F32)
        weighted_hi = under_probs("weighted_hi", [P, 2, COLS], F32R)
        weighted_lo = under_probs("weighted_lo", [P, 2, COLS], F32R)

        ctx_t = sb("ctx_t", [P, KT, B], F32)
        denom = sb("denom", [P, B], F32)
        cat_hi = sb("cat_hi", [P, CT, B], F32R)
        cat_lo = sb("cat_lo", [P, CT, B], F32R)
        item = sb("item", [P, PIECES, PIECE, CHUNK], F32)
        item_hi, under_item_hi = shared("item_hi", [P, PIECES, PIECE, CHUNK], F32R)
        item_lo, under_item_lo = shared("item_lo", [P, PIECES, PIECE, CHUNK], F32R)
        last = under_item_hi("last", [P, KT, B], F32)
        ue_raw = under_item_lo("ue_raw", [P, KT, H], F32)
        masks = sb("masks", [P, RT, CHUNK], BF16)
        raw_logits = sb("raw_logits", [P, RT, CHUNK], F32)

        attn = sb("attn", [P, 2, COLS], F32)
        ones_f = sb("ones_f", [P, P], F32)
        ones = sb("ones", [P, P], F32R)
        ve = sb("ve", [P, KT], F32)
        q_now = sb("q_now", [P, KT, BODY_ROWS], F32)
        ctx_now = sb("ctx_now", [P, KT, BODY_ROWS], F32)
        denom_now = sb("denom_now", [P, BODY_ROWS], F32)
        neg_max = sb("neg_max", [P, 2, STEP_ROWS], F32)

        hist_i = under_item_lo("hist_i", [P, ROW_TILES, HIST], I32)
        hist_f = under_item_lo("hist_f", [P, ROW_TILES, HIST], F32)
        hist_t = under_item_lo("hist_t", [P, ROW_TILES, HIST], F32)
        row_base = under_item_lo("row_base", [P, ROW_TILES, HIST], F32)
        where = sb("where", [P, COLUMNS], U32)
        where_now = sb("where_now", [P, SLOTS], U32)
        where_body = sb("where_body", [P, SLOTS], U32)
        zero = sb("zero", [P, 1], U32)
        masked_const = sb("masked_const", [P, 1], BF16)

        chunk_neg_max = sb("chunk_neg_max", [P, HALVES, RT, CHUNKS], F32)
        chunk_sum = sb("chunk_sum", [P, HALVES, RT, CHUNKS], F32)
        chunk_factor = sb("chunk_factor", [P, HALVES, RT, CHUNKS], F32)
        chunk_scale = sb("chunk_scale", [P, HALVES, RT, CHUNKS], F32)
        row_neg_max = sb("row_neg_max", [P, HALVES, RT], F32)
        row_sum = sb("row_sum", [P, HALVES, RT], F32)
        row_rec = sb("row_rec", [P, HALVES, RT], F32)
        junk = sb("junk", [P, HALVES, RT, CHUNKS], F32)

        k_ps = ctx.enter_context(nc.psum_tensor("k_ps", [P, KT, 512], F32))
        score_ps = ctx.enter_context(nc.psum_tensor("score_ps", [P, 2, 512], F32))
        logit_ps = ctx.enter_context(nc.psum_tensor("logit_ps", [P, RT, 512], F32))

        we_loaded = sem("we_loaded")
        ue_loaded = sem("ue_loaded")
        ve_loaded = sem("ve_loaded")
        last_loaded = sem("last_loaded")
        hist_loaded = sem("hist_loaded")
        x_loaded = [sem(f"x_loaded{s}") for s in range(SLOTS)]
        ones_set = sem("ones_set")
        zeros_set = sem("zeros_set")
        mask_zeroed = sem("mask_zeroed")
        where_step = sem("where_step")
        where_copied = sem("where_copied")
        scattered = sem("scattered")
        mask_complete = sem("mask_complete")
        q_made = sem("q_made")
        q_copied = sem("q_copied")
        q_staged = sem("q_staged")
        ue_hi_made = sem("ue_hi_made")
        ue_lo_made = sem("ue_lo_made")
        x_hi_made = sem("x_hi_made")
        x_lo_made = sem("x_lo_made")
        keys_made = sem("keys_made")
        tanh_made = sem("tanh_made")
        weighted_made = sem("weighted_made")
        weighted_hi_made = sem("weighted_hi_made")
        weighted_lo_made = sem("weighted_lo_made")
        scores_made = sem("scores_made")
        neg_max_made = sem("neg_max_made")
        attn_made = sem("attn_made")
        ctx_made = sem("ctx_made")
        ctx_copied = sem("ctx_copied")
        denom_ready = sem("denom_ready")
        ctx_scaled = sem("ctx_scaled")
        cat_hi_made = sem("cat_hi_made")
        cat_lo_made = sem("cat_lo_made")
        item_loaded = [sem(f"item_loaded{p}") for p in range(PIECES)]
        item_hi_made = [sem(f"item_hi_made{p}") for p in range(PIECES)]
        item_lo_made = [sem(f"item_lo_made{p}") for p in range(PIECES)]
        mask_loaded = [sem(f"mask_loaded{r}") for r in range(RT)]
        logits_made = [sem(f"logits_made{r}") for r in range(RT)]
        item_used = [sem(f"item_used{p}") for p in range(PIECES - 1)] + [logits_made[RT - 1]]
        logits_out = [sem(f"logits_out{r}") for r in range(RT)]
        neg_made = [sem(f"neg_made{r}") for r in range(RT)]
        exp_made = [sem(f"exp_made{r}") for r in range(RT)]
        row_max_made = sem("row_max_made")
        factor_made = sem("factor_made")
        sum_made = sem("sum_made")
        rec_made = sem("rec_made")
        scale_made = sem("scale_made")
        scaled_pool = sem("scaled_pool")
        scaled_dve = sem("scaled_dve")
        scaled_act = sem("scaled_act")
        stored_a = sem("stored_a")
        stored_sp = sem("stored_sp")
        stored_act = sem("stored_act")

        out_halves = out.rearrange("(h r p) i -> h p r i", h=HALVES, r=RT)

        def rows_of(half, rt):
            return slice((half * RT + rt) * P, (half * RT + rt + 1) * P)

        block = ctx.enter_context(nc.Block())

        @block.sync
        def _(sp):
            sp.dma_start(x[0][:], x_l[0]).then_inc(x_loaded[0], 16)
            sp.dma_start(last[:], last_l).then_inc(last_loaded, 16)
            sp.dma_start(x[1][:], x_l[1]).then_inc(x_loaded[1], 16)
            sp.dma_start(hist_i[:], hist.rearrange("(r p) j -> p r j", p=P)).then_inc(hist_loaded, 16)
            for s in range(2, SLOTS):
                sp.dma_start(x[s][:], x_l[s]).then_inc(x_loaded[s], 16)
            sp.wait_ge(zeros_set, 1)
            zeros = item[:].rearrange("p a b c -> p (a b c)").bitcast(BF16)
            width = ITEMS // 2
            for r in range(ROW_TILES):
                for c in range(2):
                    sp.dma_start(mask_rows[r * P:(r + 1) * P, c * width:(c + 1) * width],
                                 zeros[:, 0:width]).then_inc(mask_zeroed, 16)
            with sp.Fori(1, BODIES) as i:
                for u in range(SLOTS):
                    sp.wait_ge(ctx_made, (i * SLOTS + (u + 1 - SLOTS)) * STEP_ROWS)
                    sp.dma_start(x[u][:], x_l[i * SLOTS + u]).then_inc(x_loaded[u], 16)
            sp.wait_ge(mask_zeroed, 16 * 2 * ROW_TILES)
            for pc in range(PIECES):
                sp.dma_start(item[:, pc], items_l[0, pc]).then_inc(item_loaded[pc], 16)
            for half in range(HALVES):
                with sp.Fori(1 if half == 0 else 0, CHUNKS) as c:
                    for pc in range(PIECES):
                        sp.wait_ge(item_hi_made[pc], c + half * CHUNKS)
                        sp.wait_ge(item_lo_made[pc], c + half * CHUNKS)
                        sp.dma_start(item[:, pc], items_l[c, pc]).then_inc(item_loaded[pc], 16)
            for g in range(GROUPS):
                sp.wait_ge(scaled_dve, g + 1)
                cols = slice(g * GROUP * CHUNK, (g + 1) * GROUP * CHUNK)
                sp.dma_start(out[rows_of(HALVES - 1, 0), cols], probs[:, 0, cols]).then_inc(stored_sp, 16)
            sp.wait_ge(stored_sp, 16 * GROUPS)

        @block.gpsimd
        def _(pool):
            nc.gpsimd.memset(item[:], 0.0).then_inc(zeros_set, 1)
            nc.gpsimd.memset(ones_f[:], 1.0).then_inc(ones_set, 1)
            nc.gpsimd.memset(masked_const[:], MASKED).then_inc(where_step, 1)
            nc.gpsimd.memset(zero[:], 0).then_inc(where_step, 1)
            for r in range(ROW_TILES):
                nc.gpsimd.iota(row_base[:, r], pattern=[[0, HIST]], base=r * P * ITEMS,
                               channel_multiplier=ITEMS,
                               allow_small_or_imprecise_dtypes=True).then_inc(where_step, 1)
            done = [2 + ROW_TILES]

            def link(instruction):
                instruction.then_inc(where_step, 1)
                done[0] += 1
                pool.wait_ge(where_step, done[0])

            outside = float(B * ITEMS + 1)
            pool.wait_ge(hist_loaded, 16)
            link(nc.gpsimd.tensor_scalar(hist_t[:], hist_i[:], 0.0, float(ITEMS), ALU.is_lt, ALU.mult))
            link(nc.gpsimd.tensor_copy(hist_f[:], hist_i[:]))
            link(nc.gpsimd.tensor_tensor(hist_f[:], hist_f[:], hist_t[:], ALU.add))
            link(nc.gpsimd.tensor_scalar(hist_t[:], hist_f[:], 0.0, None, ALU.is_ge))
            link(nc.gpsimd.tensor_tensor(row_base[:], row_base[:], hist_f[:], ALU.add))
            link(nc.gpsimd.tensor_scalar(hist_f[:], hist_f[:], float(ITEMS), None, ALU.is_lt))
            link(nc.gpsimd.tensor_tensor(hist_t[:], hist_t[:], hist_f[:], ALU.mult))
            link(nc.gpsimd.tensor_scalar(row_base[:], row_base[:], -outside, None, ALU.add))
            link(nc.gpsimd.tensor_tensor(row_base[:], row_base[:], hist_t[:], ALU.mult))
            link(nc.gpsimd.tensor_scalar(where[:], row_base[:].rearrange("p r j -> p (r j)"),
                                         outside, None, ALU.add))

            def stage_q(i):
                rows = slice(i * BODY_ROWS, (i + 1) * BODY_ROWS) if isinstance(i, int) \
                    else bass.ds(i * BODY_ROWS, BODY_ROWS)
                nc.gpsimd.tensor_copy(q_now[:], q_t[:, :, rows]).then_inc(q_staged, 1)

            pool.wait_ge(q_copied, KT)
            stage_q(0)
            pool.wait_ge(mask_zeroed, 16 * 2 * ROW_TILES)

            def copies(i, last_body=False):
                if not last_body:
                    pool.wait_ge(tanh_made, (i + 1) * (SLOTS * KT))
                    stage_q(i + 1)
                pool.wait_ge(ctx_made, (i + 1) * (SLOTS * STEP_ROWS))
                rows = bass.ds(i * BODY_ROWS, BODY_ROWS)
                nc.gpsimd.tensor_copy(ctx_t[:, :, rows], ctx_now[:])
                nc.gpsimd.tensor_copy(denom[:, rows], denom_now[:]).then_inc(ctx_copied, 1)

            last_place = nc.gpsimd.to_reg(B * ITEMS - 1)
            with pool.Fori(0, SCATTER_BODIES) as i:
                nc.gpsimd.tensor_copy(where_body[:], where[:, bass.ds(i * SLOTS, SLOTS)]).then_inc(where_copied, 1)
                pool.wait_ge(where_copied, 1)
                for s in range(SLOTS):
                    nc.gpsimd.tensor_tensor(where_now[:, s:s + 1], where_body[:, s:s + 1], zero[:],
                                            ALU.add).then_inc(where_copied, 1)
                    pool.wait_ge(where_copied, 2 + s)
                    nc.gpsimd.indirect_dma_start(
                        out=mask_bias, out_offset=bass.IndirectOffsetOnAxis(ap=where_now[:, s:s + 1], axis=0),
                        in_=masked_const[:], in_offset=None,
                        bounds_check=last_place, oob_is_err=False).then_inc(scattered, 16)
                    pool.wait_ge(scattered, i * (16 * SLOTS) + 16 * (s + 1))
                copies(i)
                pool.sem_clear(where_copied)
            pool.sem_inc(mask_complete, 1)
            with pool.Fori(SCATTER_BODIES, BODIES - 1) as i:
                copies(i)
            copies(BODIES - 1, last_body=True)

            pool.wait_ge(scale_made, RT)
            for g in range(GROUPS):
                for r in range(RT):
                    p = probs[:, r].rearrange("p (c i) -> p c i", i=CHUNK)[:, g * GROUP:(g + 1) * GROUP]
                    scale = chunk_scale[:, 0, r, g * GROUP:(g + 1) * GROUP]
                    nc.gpsimd.tensor_tensor(p, p, scale.unsqueeze(2).to_broadcast([P, GROUP, CHUNK]),
                                            ALU.mult).then_inc(scaled_pool, 1)
                pool.wait_ge(scaled_pool, RT * (g + 1))
                wait(pool, stored_a, 16 * g)
                cols = slice(g * GROUP * CHUNK, (g + 1) * GROUP * CHUNK)
                pool.dma_start(out_halves[0, :, :, cols], probs[:, :, cols]).then_inc(stored_a, 16)
            pool.wait_ge(stored_a, 16 * GROUPS)

        @block.scalar
        def _(act):
            act.dma_start(ue_raw[:], ue_l).then_inc(ue_loaded, 16)
            act.dma_start(we_raw[:], we_l).then_inc(we_loaded, 16)
            act.dma_start(ve[:], ve_l).then_inc(ve_loaded, 16)
            act.wait_ge(ones_set, 1)
            nc.scalar.activation(ones[:], ones_f[:], ACT.Copy).then_inc(ones_set, 1)

            def split_x(i, u):
                act.wait_ge(x_loaded[u % SLOTS], (i + 1) * 16)
                wait(act, keys_made, (i * SLOTS + (u - 1)) * KT)
                nc.scalar.activation(x_hi[u % 2][:], x[u % SLOTS][:], ACT.Copy).then_inc(x_hi_made, 1)

            def split_weighted(i, u):
                act.wait_ge(weighted_made, (i * SLOTS + u) * KT)
                wait(act, scores_made, i * SLOTS + (u - 2))
                nc.scalar.activation(weighted_hi[:, (u - 1) % 2], weighted[:, (u - 1) % 2],
                                     ACT.Copy).then_inc(weighted_hi_made, 1)

            def attention(i, u):
                act.wait_ge(neg_max_made, i * SLOTS + u)
                wait(act, ctx_made, (i * SLOTS + (u - 2)) * STEP_ROWS)
                if u == 1:
                    wait(act, ctx_copied, i)
                for g in range(STEP_ROWS):
                    cols = slice(g * S, (g + 1) * S)
                    row = (u - 1) % SLOTS * STEP_ROWS + g
                    nc.scalar.activation(attn[:, (u - 1) % 2, cols], score_ps[:, (u - 1) % 2, cols], ACT.Exp,
                                         bias=neg_max[:, (u - 1) % 2, g:g + 1],
                                         accum_out=denom_now[:, row:row + 1]).then_inc(attn_made, 1)

            def tanh(i, u, m):
                act.wait_ge(keys_made, (i * SLOTS + u) * KT + (m + 1))
                wait(act, weighted_made, (i * SLOTS + (u - 2)) * KT + (m + 1))
                for g in range(STEP_ROWS):
                    cols = slice(g * S, (g + 1) * S)
                    row = u * STEP_ROWS + g
                    made = nc.scalar.activation(th[u % 2][:, m, cols], k_ps[:, m, cols], ACT.Tanh,
                                                bias=q_now[:, m, row:row + 1])
                made.then_inc(tanh_made, 1)

            def step(i, u, first=False, final=False):
                if not first:
                    split_weighted(i, u)
                if not final:
                    split_x(i + (u + 1) // SLOTS, (u + 1) % SLOTS)
                if u == 0:
                    act.wait_ge(q_staged, i + 1)
                tanh(i, u, 0)
                tanh(i, u, 1)
                if not first:
                    attention(i, u)
                for m in range(2, KT):
                    tanh(i, u, m)

            split_x(0, 0)
            act.wait_ge(ue_loaded, 16)
            for m in range(KT):
                nc.scalar.activation(ue_hi[:, m], ue_raw[:, m], ACT.Copy).then_inc(ue_hi_made, 1)
            for u in range(SLOTS):
                step(0, u, first=(u == 0))
                if u == 1:
                    act.wait_ge(last_loaded, 16)
                    nc.scalar.activation(cat_hi[:, 0:KT], last[:], ACT.Copy).then_inc(cat_hi_made, 1)
            with act.Fori(1, BODIES - 1) as i:
                for u in range(SLOTS):
                    step(i, u)
            for u in range(SLOTS):
                step(BODIES - 1, u, final=(u == SLOTS - 1))
            split_weighted(BODIES, 0)

            def load_mask(half, rt, c):
                act.dma_start(masks[:, rt], mask_rows[rows_of(half, rt), bass.ds(c * CHUNK, CHUNK)]) \
                   .then_inc(mask_loaded[rt], 16)

            def split_item(n, pc):
                act.wait_ge(item_loaded[pc], (n + 1) * 16)
                wait(act, item_used[pc], n)
                nc.scalar.activation(item_hi[:, pc], item[:, pc], ACT.Copy).then_inc(item_hi_made[pc], 1)

            def exponentiate(half, rt, c, next_mask=True):
                act.wait_ge(neg_made[rt], c + (half * CHUNKS + 1))
                nc.scalar.activation(probs[:, rt, bass.ds(c * CHUNK, CHUNK)], raw_logits[:, rt], ACT.Exp,
                                     bias=chunk_neg_max[:, half, rt, bass.ds(c, 1)],
                                     accum_out=chunk_sum[:, half, rt, bass.ds(c, 1)]).then_inc(exp_made[rt], 1)
                if next_mask:
                    load_mask(half, rt, c + 1)

            for pc in range(PIECES):
                split_item(0, pc)
            act.wait_ge(mask_complete, 1)
            for rt in range(RT):
                load_mask(0, rt, 0)
            attention(BODIES, 0)
            for half in range(HALVES):
                act.wait_ge(ctx_scaled, half + 1)
                cols = slice(half * HALF, (half + 1) * HALF)
                nc.scalar.activation(cat_hi[:, KT:CT, cols], ctx_t[:, :, cols], ACT.Copy).then_inc(cat_hi_made, 1)

            def chunk(half, c, last_of_half=False, last_of_all=False):
                n = c + half * CHUNKS
                if not last_of_all:
                    split_item(n + 1, 0)
                    split_item(n + 1, 1)
                exponentiate(half, 0, c, not last_of_half)
                if not last_of_all:
                    split_item(n + 1, 2)
                exponentiate(half, 1, c, not last_of_half)
                if not last_of_all:
                    split_item(n + 1, 3)

            def factors(half):
                act.wait_ge(row_max_made, half + 1)
                for rt in range(RT):
                    nc.scalar.activation(chunk_factor[:, half, rt], chunk_neg_max[:, half, rt], ACT.Exp,
                                         scale=-1.0, bias=row_neg_max[:, half, rt:rt + 1]).then_inc(factor_made, 1)

            with act.Fori(0, CHUNKS - 1) as c:
                chunk(0, c)
            chunk(0, CHUNKS - 1, last_of_half=True)
            for rt in range(RT):
                load_mask(1, rt, 0)
            factors(0)
            with act.Fori(0, GROUPS - 1) as g:
                act.wait_ge(stored_a, g * 16 + 16)
                for c in range(GROUP):
                    chunk(1, g * GROUP + c)
            act.wait_ge(stored_a, GROUPS * 16)
            for c in range(CHUNKS - GROUP, CHUNKS):
                chunk(1, c, last_of_half=(c == CHUNKS - 1), last_of_all=(c == CHUNKS - 1))
            factors(1)
            act.wait_ge(scale_made, RT * HALVES)
            for g in range(GROUPS):
                for c in range(g * GROUP, (g + 1) * GROUP):
                    p = probs[:, 1, c * CHUNK:(c + 1) * CHUNK]
                    scaled = nc.scalar.activation(p, p, ACT.Copy, scale=chunk_scale[:, 1, 1, c:c + 1])
                scaled.then_inc(scaled_act, 1)
                act.wait_ge(scaled_act, g + 1)
                cols = slice(g * GROUP * CHUNK, (g + 1) * GROUP * CHUNK)
                act.dma_start(out[rows_of(1, 1), cols], probs[:, 1, cols]).then_inc(stored_act, 16)
            act.wait_ge(stored_act, 16 * GROUPS)

        @block.vector
        def _(dve):
            def split_x(i, u):
                dve.wait_ge(x_hi_made, i * SLOTS + (u + 1))
                nc.vector.tensor_tensor(x_lo[u % 2][:], x[u % SLOTS][:], x_hi[u % 2][:].bitcast(F32),
                                        ALU.subtract).then_inc(x_lo_made, 1)

            def split_weighted(i, u):
                dve.wait_ge(weighted_hi_made, i * SLOTS + u)
                nc.vector.tensor_tensor(weighted_lo[:, (u - 1) % 2], weighted[:, (u - 1) % 2],
                                        weighted_hi[:, (u - 1) % 2].bitcast(F32),
                                        ALU.subtract).then_inc(weighted_lo_made, 1)

            def weigh(i, u, m):
                dve.wait_ge(tanh_made, (i * SLOTS + u) * KT + (m + 1))
                w = weighted[:, u % 2]
                if m == 0:
                    made = nc.vector.tensor_scalar(w, th[u % 2][:, m], ve[:, m:m + 1], None, ALU.mult)
                else:
                    dve.wait_ge(weighted_made, (i * SLOTS + u) * KT + m)
                    made = nc.vector.scalar_tensor_tensor(w, th[u % 2][:, m], ve[:, m:m + 1], w,
                                                          ALU.mult, ALU.add)
                made.then_inc(weighted_made, 1)

            def maximum(i, u):
                dve.wait_ge(scores_made, i * SLOTS + u)
                s = score_ps[:, (u - 1) % 2, 0:COLS].rearrange("p (g s) -> p g s", g=STEP_ROWS)
                wait(dve, attn_made, (i * SLOTS + (u - 2)) * STEP_ROWS)
                nc.vector.tensor_reduce(neg_max[:, (u - 1) % 2], s, AX_X, ALU.max,
                                        negate=True).then_inc(neg_max_made, 1)

            def pool_memory(i, u, g):
                dve.wait_ge(attn_made, (i * SLOTS + (u - 1)) * STEP_ROWS + (g + 1))
                if u == 1 and g == 0:
                    wait(dve, ctx_copied, i)
                cols = slice(g * S, (g + 1) * S)
                row = (u - 1) % SLOTS * STEP_ROWS + g
                for k in range(KT):
                    xs = x[(u - 1) % SLOTS][:, k, cols]
                    made = nc.vector.tensor_tensor_reduce(xs, xs, attn[:, (u - 1) % 2, cols], 1.0, 0.0, ALU.mult,
                                                          ALU.add, ctx_now[:, k, row:row + 1])
                made.then_inc(ctx_made, 1)

            def step(i, u, first=False, final=False):
                if not first:
                    split_weighted(i, u)
                if not final:
                    split_x(i + (u + 1) // SLOTS, (u + 1) % SLOTS)
                weigh(i, u, 0)
                if not first:
                    maximum(i, u)
                weigh(i, u, 1)
                weigh(i, u, 2)
                if not first:
                    pool_memory(i, u, 0)
                weigh(i, u, 3)
                if not first:
                    pool_memory(i, u, 1)

            split_x(0, 0)
            dve.wait_ge(ue_loaded, 16)
            for m in range(KT):
                dve.wait_ge(ue_hi_made, m + 1)
                nc.vector.tensor_tensor(ue_lo[:, m], ue_raw[:, m], ue_hi[:, m].bitcast(F32),
                                        ALU.subtract).then_inc(ue_lo_made, 1)
            for m in range(KT):
                dve.wait_ge(q_made, m + 1)
                nc.vector.tensor_copy(q_t[:, m], k_ps[:, m]).then_inc(q_copied, 1)
            dve.wait_ge(ve_loaded, 16)
            for u in range(SLOTS):
                step(0, u, first=(u == 0))
                if u == 1:
                    dve.wait_ge(cat_hi_made, 1)
                    nc.vector.tensor_tensor(cat_lo[:, 0:KT], last[:], cat_hi[:, 0:KT].bitcast(F32),
                                            ALU.subtract).then_inc(cat_lo_made, 1)
            with dve.Fori(1, BODIES - 1) as i:
                for u in range(SLOTS):
                    step(i, u)
            for u in range(SLOTS):
                step(BODIES - 1, u, final=(u == SLOTS - 1))
            split_weighted(BODIES, 0)

            def split_item(n, pc):
                dve.wait_ge(item_hi_made[pc], n + 1)
                nc.vector.tensor_tensor(item_lo[:, pc], item[:, pc], item_hi[:, pc].bitcast(F32),
                                        ALU.subtract).then_inc(item_lo_made[pc], 1)

            def take_logits(half, rt, c):
                n = c + half * CHUNKS
                dve.wait_ge(logits_made[rt], n + 1)
                dve.wait_ge(mask_loaded[rt], n * 16 + 16)
                wait(dve, exp_made[rt], n)
                nc.vector.tensor_tensor(raw_logits[:, rt], masks[:, rt], logit_ps[:, rt, 0:CHUNK],
                                        ALU.add).then_inc(logits_out[rt], 1)
                dve.wait_ge(logits_out[rt], n + 1)
                nc.vector.tensor_reduce(chunk_neg_max[:, half, rt, bass.ds(c, 1)], raw_logits[:, rt], AX_X,
                                        ALU.max, negate=True).then_inc(neg_made[rt], 1)

            def normalise(half):
                rows = slice(half * HALF, (half + 1) * HALF)
                c = ctx_t[:, :, rows]
                nc.vector.tensor_tensor(c, c, denom[:, rows].unsqueeze(1).to_broadcast([P, KT, HALF]),
                                        ALU.mult).then_inc(ctx_scaled, 1)

            def split_ctx(half):
                rows = slice(half * HALF, (half + 1) * HALF)
                dve.wait_ge(cat_hi_made, half + 2)
                nc.vector.tensor_tensor(cat_lo[:, KT:CT, rows], ctx_t[:, :, rows],
                                        cat_hi[:, KT:CT, rows].bitcast(F32), ALU.subtract).then_inc(cat_lo_made, 1)

            for pc in range(PIECES):
                split_item(0, pc)
            maximum(BODIES, 0)
            for g in range(STEP_ROWS):
                pool_memory(BODIES, 0, g)
            dve.wait_ge(ctx_copied, BODIES)
            nc.vector.reciprocal(denom[:], denom[:]).then_inc(denom_ready, 1)
            dve.wait_ge(denom_ready, 1)
            for half in range(HALVES):
                normalise(half)
            for half in range(HALVES):
                split_ctx(half)

            def chunk(half, c, last_of_all=False):
                n = c + half * CHUNKS
                if not last_of_all:
                    split_item(n + 1, 0)
                    split_item(n + 1, 1)
                take_logits(half, 0, c)
                if not last_of_all:
                    split_item(n + 1, 2)
                take_logits(half, 1, c)
                if not last_of_all:
                    split_item(n + 1, 3)

            def scales(half):
                for rt in range(RT):
                    dve.wait_ge(neg_made[rt], (half + 1) * CHUNKS)
                nc.vector.tensor_reduce(row_neg_max[:, half], chunk_neg_max[:, half], AX_X,
                                        ALU.min).then_inc(row_max_made, 1)
                dve.wait_ge(factor_made, RT * (half + 1))
                for rt in range(RT):
                    dve.wait_ge(exp_made[rt], (half + 1) * CHUNKS)
                    nc.vector.tensor_tensor_reduce(junk[:, half, rt], chunk_factor[:, half, rt],
                                                   chunk_sum[:, half, rt], 1.0, 0.0, ALU.mult, ALU.add,
                                                   row_sum[:, half, rt:rt + 1]).then_inc(sum_made, 1)
                dve.wait_ge(sum_made, RT * (half + 1))
                nc.vector.reciprocal(row_rec[:, half], row_sum[:, half]).then_inc(rec_made, 1)
                dve.wait_ge(rec_made, half + 1)
                for rt in range(RT):
                    nc.vector.tensor_scalar(chunk_scale[:, half, rt], chunk_factor[:, half, rt],
                                            row_rec[:, half, rt:rt + 1], None, ALU.mult).then_inc(scale_made, 1)

            chunk(0, 0)
            with dve.Fori(1, CHUNKS) as c:
                chunk(0, c)
            scales(0)
            with dve.Fori(0, CHUNKS - 1) as c:
                chunk(1, c)
            chunk(1, CHUNKS - 1, last_of_all=True)
            scales(1)
            dve.wait_ge(scale_made, RT * HALVES)
            for g in range(GROUPS):
                for c in range(g * GROUP, (g + 1) * GROUP):
                    p = probs[:, 0, c * CHUNK:(c + 1) * CHUNK]
                    scaled = nc.vector.tensor_scalar(p, p, chunk_scale[:, 1, 0, c:c + 1], None, ALU.mult)
                scaled.then_inc(scaled_dve, 1)

        @block.tensor
        def _(pe):
            pe.wait_ge(we_loaded, 16)
            pe.wait_ge(last_loaded, 16)
            for m in range(KT):
                for k in range(KT):
                    made = nc.tensor.matmul(k_ps[:, m, :], we_raw[:, k, m * P:(m + 1) * P], last[:, k],
                                            start=(k == 0), stop=(k == KT - 1))
                made.then_inc(q_made, 1)

            def keys(i, u, m):
                if isinstance(i, int) and i == 0 and u == 0:
                    pe.wait_ge(q_copied, m + 1)
                wait(pe, tanh_made, (i * SLOTS + (u - 1)) * KT + (m + 1))
                hi, lo = x_hi[u % 2], x_lo[u % 2]
                for k in range(KT):
                    w = slice(m * P, (m + 1) * P)
                    for n, (weights, moving) in enumerate(((ue_hi, hi), (ue_hi, lo), (ue_lo, hi))):
                        made = nc.tensor.matmul(k_ps[:, m, 0:COLS], weights[:, k, w], moving[:, k],
                                                start=(k == 0 and n == 0), stop=(k == KT - 1 and n == 2))
                made.then_inc(keys_made, 1)

            def scores(i, u):
                pe.wait_ge(weighted_hi_made, i * SLOTS + u)
                pe.wait_ge(weighted_lo_made, i * SLOTS + u)
                wait(pe, attn_made, (i * SLOTS + (u - 2)) * STEP_ROWS)
                b = (u - 1) % 2
                nc.tensor.matmul(score_ps[:, b, 0:COLS], ones[:], weighted_hi[:, b], start=True, stop=False)
                nc.tensor.matmul(score_ps[:, b, 0:COLS], ones[:], weighted_lo[:, b], start=False,
                                 stop=True).then_inc(scores_made, 1)

            def step(i, u, first=False):
                pe.wait_ge(x_hi_made, i * SLOTS + (u + 1))
                pe.wait_ge(x_lo_made, i * SLOTS + (u + 1))
                keys(i, u, 0)
                keys(i, u, 1)
                if not first:
                    scores(i, u)
                keys(i, u, 2)
                keys(i, u, 3)

            pe.wait_ge(ones_set, 2)
            pe.wait_ge(ue_hi_made, KT)
            pe.wait_ge(ue_lo_made, KT)
            for u in range(SLOTS):
                step(0, u, first=(u == 0))
            with pe.Fori(1, BODIES) as i:
                for u in range(SLOTS):
                    step(i, u)
            scores(BODIES, 0)

            def products(half, c, pieces, rt, n):
                for pc in pieces:
                    for k in range(PIECE):
                        tile = pc * PIECE + k
                        w = slice((half * RT + rt) * P, (half * RT + rt + 1) * P)
                        for a, (weights, moving) in enumerate(((cat_hi, item_hi), (cat_hi, item_lo),
                                                               (cat_lo, item_hi))):
                            made = nc.tensor.matmul(logit_ps[:, rt, 0:CHUNK], weights[:, tile, w], moving[:, pc, k],
                                                    start=(tile == 0 and a == 0), stop=(tile == CT - 1 and a == 2))
                    if rt == RT - 1:
                        made.then_inc(item_used[pc], 1)
                return made

            def chunk(half, c, first=False):
                n = c + half * CHUNKS
                for part in range(2):
                    pieces = range(part * PIECES // 2, (part + 1) * PIECES // 2)
                    if first:
                        pe.wait_ge(cat_hi_made, 1 + part * HALVES)
                        pe.wait_ge(cat_lo_made, 1 + part * HALVES)
                    for pc in pieces:
                        pe.wait_ge(item_hi_made[pc], n + 1)
                        pe.wait_ge(item_lo_made[pc], n + 1)
                    for rt in range(RT):
                        if part == 0:
                            wait(pe, logits_out[rt], n)
                        made = products(half, c, pieces, rt, n)
                        if part == 1 and rt < RT - 1:
                            made.then_inc(logits_made[rt], 1)

            chunk(0, 0, first=True)
            with pe.Fori(1, CHUNKS) as c:
                chunk(0, c)
            with pe.Fori(0, CHUNKS) as c:
                chunk(1, c)


def kernel(r_last_memory, r_all_memory, r_mask, L0_rec_item_matrix_transpose, L0_rec_We, L0_rec_Ue, L0_rec_Ve):
    import concourse.bacc as bacc
    from concourse.bass_utils import run_bass_kernel_spmd

    B, S, H = r_all_memory.shape
    ITEMS = L0_rec_item_matrix_transpose.shape[1]
    KT = H // P
    chunks = ITEMS // CHUNK

    def features_first(w):
        return np.ascontiguousarray(np.asarray(w).reshape(-1, KT, P).transpose(2, 1, 0))

    x = np.asarray(r_all_memory).reshape(B // STEP_ROWS, STEP_ROWS * S, KT, P).transpose(0, 3, 2, 1)
    items = np.asarray(L0_rec_item_matrix_transpose).reshape(2, H, chunks, CHUNK)[::-1]
    items = items.reshape(2 * KT // PIECE, PIECE, P, chunks, CHUNK).transpose(3, 0, 2, 1, 4)
    arrays = {
        "x_l": np.ascontiguousarray(x),
        "last_l": features_first(r_last_memory),
        "we_l": features_first(L0_rec_We),
        "ue_l": features_first(L0_rec_Ue),
        "ve_l": features_first(L0_rec_Ve)[:, :, 0],
        "items_l": np.ascontiguousarray(items),
        "hist": np.ascontiguousarray(np.asarray(r_mask)),
    }
    nc = bacc.Bacc("TRN2", target_bir_lowering=False, num_devices=1)
    args = {name: nc.dram_tensor(name, a.shape, mybir.dt.from_np(a.dtype), kind="ExternalInput").ap()
            for name, a in arrays.items()}
    out = nc.dram_tensor("probs_out", (B, ITEMS), F32, kind="ExternalOutput").ap()
    attention_rank(nc, out=out, **args)
    result = run_bass_kernel_spmd(nc, [arrays], core_ids=[0])
    return result.results[0]["probs_out"]
```

```python
from contextlib import ExitStack

import numpy as np
import concourse.bass as bass
from concourse import mybir

ALU = mybir.AluOpType
ACT = mybir.ActivationFunctionType
AX_X = mybir.AxisListType.X
F32 = mybir.dt.float32
F32R = mybir.dt.float32r
BF16 = mybir.dt.bfloat16
I32 = mybir.dt.int32
U32 = mybir.dt.uint32

P = 128
MASKED = -1000000000.0
STEP_ROWS = 2
SLOTS = 4
CHUNK = 500
PIECE = 2
GROUP = 5
STORE_EVERY = 3


def wait(eng, sem, count):
    if not isinstance(count, int) or count > 0:
        eng.wait_ge(sem, count)


def attention_rank(nc, x_l, last_l, we_l, ue_l, ve_l, items_l, hist, out):
    STEPS, _, KT, COLS = x_l.shape
    S = COLS // STEP_ROWS
    B = last_l.shape[2]
    H = KT * P
    BODIES = STEPS // SLOTS
    BODY_ROWS = SLOTS * STEP_ROWS
    CHUNKS, PIECES = items_l.shape[0:2]
    ITEMS = CHUNKS * CHUNK
    HIST = hist.shape[1]
    ROW_TILES = B // P
    HALVES = 2
    RT = ROW_TILES // HALVES
    HALF = RT * P
    GROUPS = CHUNKS // GROUP
    CT = PIECES * PIECE
    COLUMNS = ROW_TILES * HIST
    SCATTER_BODIES = COLUMNS // SLOTS
    ZERO_PARTS = 2
    ZERO_BODIES = ROW_TILES * ZERO_PARTS // SLOTS
    SCATTER_FROM = ZERO_BODIES + 3
    assert B == STEPS * STEP_ROWS == BODIES * BODY_ROWS and CHUNKS == GROUPS * GROUP
    assert CT == 2 * KT and SLOTS == KT and SCATTER_BODIES * SLOTS == COLUMNS and SCATTER_FROM + SCATTER_BODIES < BODIES

    mask_bias = nc.dram_tensor("mask_bias", (B * ITEMS, 1), BF16, kind="Internal").ap()
    mask_rows = mask_bias.rearrange("(b i) o -> b (i o)", b=B)

    with ExitStack() as ctx:
        def sb(name, shape, dt):
            return ctx.enter_context(nc.sbuf_tensor(name, shape, dt))

        def sem(name):
            return ctx.enter_context(nc.semaphore(name))

        def shared(name, shape, dt):
            start = -(-nc.sbuf_base // 32) * 32
            tensor = sb(name, shape, dt)
            taken = [start]

            def under(name, shape, dt):
                at = taken[0]
                taken[0] = at + 4 * int(np.prod(shape[1:]))
                assert taken[0] <= start + 4 * int(np.prod(tensor.shape[1:]))
                return nc.alloc_sbuf_tensor_at(name, shape, dt, offset=at)
            return tensor, under

        we_at = -(-nc.sbuf_base // 32) * 32
        probs, under_probs = shared("probs", [P, RT, ITEMS], F32)
        th = [under_probs(f"th{s}", [P, KT, COLS], F32) for s in range(2)]
        we_raw = nc.alloc_sbuf_tensor_at("we_raw", [P, KT, H], F32, offset=we_at)

        x = [under_probs(f"x{s}", [P, KT, COLS], F32) for s in range(SLOTS)]
        x_hi = [under_probs(f"x_hi{s}", [P, KT, COLS], F32R) for s in range(2)]
        x_lo = [under_probs(f"x_lo{s}", [P, KT, COLS], F32R) for s in range(2)]
        ue_hi = under_probs("ue_hi", [P, KT, H], F32R)
        ue_lo = under_probs("ue_lo", [P, KT, H], F32R)
        q_t = under_probs("q_t", [P, KT, B], F32)
        weighted = under_probs("weighted", [P, 2, COLS], F32)
        weighted_hi = under_probs("weighted_hi", [P, 2, COLS], F32R)
        weighted_lo = under_probs("weighted_lo", [P, 2, COLS], F32R)

        cat_hi = sb("cat_hi", [P, CT, B], F32R)
        cat_lo = sb("cat_lo", [P, CT, B], F32R)
        item = sb("item", [P, PIECES, PIECE, CHUNK], F32)
        item_hi, under_item_hi = shared("item_hi", [P, PIECES, PIECE, CHUNK], F32R)
        item_lo, under_item_lo = shared("item_lo", [P, PIECES, PIECE, CHUNK], F32R)
        last = under_item_hi("last", [P, KT, B], F32)
        ue_raw = under_item_lo("ue_raw", [P, KT, H], F32)
        masks = sb("masks", [P, RT, CHUNK], BF16)
        raw_logits = sb("raw_logits", [P, RT, CHUNK], F32)

        attn = sb("attn", [P, 2, COLS], F32)
        ones_f = sb("ones_f", [P, P], F32)
        ones = sb("ones", [P, P], F32R)
        ve = sb("ve", [P, KT], F32)
        q_now = sb("q_now", [P, KT, BODY_ROWS], F32)
        ctx_now = sb("ctx_now", [P, KT, BODY_ROWS], F32)
        denom_now = sb("denom_now", [P, BODY_ROWS], F32)
        denom_rec = sb("denom_rec", [P, BODY_ROWS], F32)
        ctx_norm = sb("ctx_norm", [P, KT, BODY_ROWS], F32)
        ctx_hi = sb("ctx_hi", [P, KT, BODY_ROWS], F32R)
        neg_max = sb("neg_max", [P, 2, STEP_ROWS], F32)

        hist_i = under_item_lo("hist_i", [P, ROW_TILES, HIST], I32)
        hist_f = under_item_lo("hist_f", [P, ROW_TILES, HIST], F32)
        hist_t = under_item_lo("hist_t", [P, ROW_TILES, HIST], F32)
        row_base = under_item_lo("row_base", [P, ROW_TILES, HIST], F32)
        where = sb("where", [P, COLUMNS], U32)
        where_now = sb("where_now", [P, SLOTS], U32)
        where_body = sb("where_body", [P, SLOTS], U32)
        zero = sb("zero", [P, 1], U32)
        masked_const = sb("masked_const", [P, 1], BF16)

        chunk_neg_max = sb("chunk_neg_max", [P, HALVES, RT, CHUNKS], F32)
        chunk_sum = sb("chunk_sum", [P, HALVES, RT, CHUNKS], F32)
        chunk_factor = sb("chunk_factor", [P, HALVES, RT, CHUNKS], F32)
        chunk_scale = sb("chunk_scale", [P, HALVES, RT, CHUNKS], F32)
        row_neg_max = sb("row_neg_max", [P, HALVES, RT], F32)
        row_sum = sb("row_sum", [P, HALVES, RT], F32)
        row_rec = sb("row_rec", [P, HALVES, RT], F32)
        factor_times_sum = sb("factor_times_sum", [P, HALVES, RT, CHUNKS], F32)

        k_ps = ctx.enter_context(nc.psum_tensor("k_ps", [P, KT, 512], F32))
        score_ps = ctx.enter_context(nc.psum_tensor("score_ps", [P, 2, 512], F32))
        logit_ps = ctx.enter_context(nc.psum_tensor("logit_ps", [P, RT, 512], F32))

        we_loaded = [sem(f"we_loaded{k}") for k in range(KT)]
        ue_loaded = sem("ue_loaded")
        ve_loaded = sem("ve_loaded")
        last_loaded = [sem(f"last_loaded{k}") for k in range(KT)]
        hist_loaded = sem("hist_loaded")
        x_loaded = [sem(f"x_loaded{s}") for s in range(SLOTS)]
        ones_set = sem("ones_set")
        zeros_set = sem("zeros_set")
        mask_zeroed = sem("mask_zeroed")
        where_step = sem("where_step")
        where_copied = sem("where_copied")
        scattered = sem("scattered")
        mask_complete = sem("mask_complete")
        q_made = sem("q_made")
        q_copied = sem("q_copied")
        q_staged = sem("q_staged")
        ue_hi_made = sem("ue_hi_made")
        ue_lo_made = sem("ue_lo_made")
        x_hi_made = sem("x_hi_made")
        x_lo_made = sem("x_lo_made")
        keys_made = sem("keys_made")
        tanh_made = sem("tanh_made")
        weighed_first = sem("weighed_first")
        weighted_made = sem("weighted_made")
        weighted_hi_made = sem("weighted_hi_made")
        weighted_lo_made = sem("weighted_lo_made")
        scores_made = sem("scores_made")
        neg_max_made = sem("neg_max_made")
        attn_made = sem("attn_made")
        ctx_made = sem("ctx_made")
        denom_rec_made = sem("denom_rec_made")
        ctx_normalised = sem("ctx_normalised")
        ctx_hi_made = sem("ctx_hi_made")
        ctx_split = sem("ctx_split")
        cat_hi_made = sem("cat_hi_made")
        cat_lo_made = sem("cat_lo_made")
        item_loaded = [sem(f"item_loaded{p}") for p in range(PIECES)]
        item_hi_made = [sem(f"item_hi_made{p}") for p in range(PIECES)]
        item_lo_made = [sem(f"item_lo_made{p}") for p in range(PIECES)]
        mask_loaded = [sem(f"mask_loaded{r}") for r in range(RT)]
        logits_made = [sem(f"logits_made{r}") for r in range(RT)]
        item_used = [sem(f"item_used{p}") for p in range(PIECES - 1)] + [logits_made[RT - 1]]
        logits_out = [sem(f"logits_out{r}") for r in range(RT)]
        neg_made = [sem(f"neg_made{r}") for r in range(RT)]
        exp_made = [sem(f"exp_made{r}") for r in range(RT)]
        row_max_made = sem("row_max_made")
        factor_made = sem("factor_made")
        sum_made = sem("sum_made")
        rec_made = sem("rec_made")
        scale_made = sem("scale_made")
        scaled_pool = sem("scaled_pool")
        scaled_dve = sem("scaled_dve")
        scaled_act = sem("scaled_act")
        stored_a = sem("stored_a")
        stored_sp = sem("stored_sp")
        stored_act = sem("stored_act")

        out_halves = out.rearrange("(h r p) i -> h p r i", h=HALVES, r=RT)

        def rows_of(half, rt):
            return slice((half * RT + rt) * P, (half * RT + rt + 1) * P)

        block = ctx.enter_context(nc.Block())

        @block.sync
        def _(sp):
            for k in range(KT):
                sp.dma_start(last[:, k], last_l[:, k]).then_inc(last_loaded[k], 16)
            sp.dma_start(x[0][:], x_l[0]).then_inc(x_loaded[0], 16)
            sp.dma_start(x[1][:], x_l[1]).then_inc(x_loaded[1], 16)
            sp.dma_start(hist_i[:], hist.rearrange("(r p) j -> p r j", p=P)).then_inc(hist_loaded, 16)
            for s in range(2, SLOTS):
                sp.dma_start(x[s][:], x_l[s]).then_inc(x_loaded[s], 16)

            def load_x(i, u):
                sp.wait_ge(ctx_made, (i * SLOTS + (u + 1 - SLOTS)) * STEP_ROWS)
                sp.dma_start(x[u][:], x_l[i * SLOTS + u]).then_inc(x_loaded[u], 16)

            sp.wait_ge(zeros_set, 1)
            zeros = item[:].rearrange("p a b c -> p (a b c)").bitcast(BF16)
            width = ITEMS // ZERO_PARTS
            for n in range(ROW_TILES * ZERO_PARTS):
                load_x(1 + n // SLOTS, n % SLOTS)
                r, c = divmod(n, ZERO_PARTS)
                sp.dma_start(mask_rows[r * P:(r + 1) * P, c * width:(c + 1) * width],
                             zeros[:, 0:width]).then_inc(mask_zeroed, 16)
            with sp.Fori(1 + ZERO_BODIES, BODIES) as i:
                for u in range(SLOTS):
                    load_x(i, u)
            sp.wait_ge(mask_zeroed, 16 * ZERO_PARTS * ROW_TILES)
            for pc in range(PIECES):
                sp.dma_start(item[:, pc], items_l[0, pc]).then_inc(item_loaded[pc], 16)
            for half in range(HALVES):
                with sp.Fori(1 if half == 0 else 0, CHUNKS) as c:
                    for pc in range(PIECES):
                        sp.wait_ge(item_hi_made[pc], c + half * CHUNKS)
                        sp.wait_ge(item_lo_made[pc], c + half * CHUNKS)
                        sp.dma_start(item[:, pc], items_l[c, pc]).then_inc(item_loaded[pc], 16)
            for g in range(GROUPS):
                sp.wait_ge(scaled_dve, g + 2)
                cols = slice(g * GROUP * CHUNK, (g + 1) * GROUP * CHUNK)
                sp.dma_start(out[rows_of(HALVES - 1, 0), cols], probs[:, 0, cols]).then_inc(stored_sp, 16)
            sp.wait_ge(stored_sp, 16 * GROUPS)

        @block.gpsimd
        def _(pool):
            nc.gpsimd.memset(item[:], 0.0).then_inc(zeros_set, 1)
            nc.gpsimd.memset(ones_f[:], 1.0).then_inc(ones_set, 1)
            nc.gpsimd.memset(ctx_norm[:], 0.0).then_inc(ctx_split, 1)
            nc.gpsimd.memset(masked_const[:], MASKED).then_inc(where_step, 1)
            nc.gpsimd.memset(zero[:], 0).then_inc(where_step, 1)
            for r in range(ROW_TILES):
                nc.gpsimd.iota(row_base[:, r], pattern=[[0, HIST]], base=r * P * ITEMS,
                               channel_multiplier=ITEMS,
                               allow_small_or_imprecise_dtypes=True).then_inc(where_step, 1)
            done = [2 + ROW_TILES]

            def link(instruction):
                instruction.then_inc(where_step, 1)
                done[0] += 1
                pool.wait_ge(where_step, done[0])

            outside = float(B * ITEMS + 1)
            pool.wait_ge(hist_loaded, 16)
            link(nc.gpsimd.tensor_scalar(hist_t[:], hist_i[:], 0.0, float(ITEMS), ALU.is_lt, ALU.mult))
            link(nc.gpsimd.tensor_copy(hist_f[:], hist_i[:]))
            link(nc.gpsimd.tensor_tensor(hist_f[:], hist_f[:], hist_t[:], ALU.add))
            link(nc.gpsimd.tensor_scalar(hist_t[:], hist_f[:], 0.0, None, ALU.is_ge))
            link(nc.gpsimd.tensor_tensor(row_base[:], row_base[:], hist_f[:], ALU.add))
            link(nc.gpsimd.tensor_scalar(hist_f[:], hist_f[:], float(ITEMS), None, ALU.is_lt))
            link(nc.gpsimd.tensor_tensor(hist_t[:], hist_t[:], hist_f[:], ALU.mult))
            link(nc.gpsimd.tensor_scalar(row_base[:], row_base[:], -outside, None, ALU.add))
            link(nc.gpsimd.tensor_tensor(row_base[:], row_base[:], hist_t[:], ALU.mult))
            link(nc.gpsimd.tensor_scalar(where[:], row_base[:].rearrange("p r j -> p (r j)"),
                                         outside, None, ALU.add))

            def stage_q(i):
                rows = slice(i * BODY_ROWS, (i + 1) * BODY_ROWS) if isinstance(i, int) \
                    else bass.ds(i * BODY_ROWS, BODY_ROWS)
                nc.gpsimd.tensor_copy(q_now[:], q_t[:, :, rows]).then_inc(q_staged, 1)

            pool.wait_ge(q_copied, KT)
            stage_q(0)

            def copies(i, last_body=False):
                if not last_body:
                    pool.wait_ge(tanh_made, (i + 1) * (SLOTS * KT))
                    stage_q(i + 1)
                rows = bass.ds(i * BODY_ROWS, BODY_ROWS)
                pool.wait_ge(ctx_hi_made, i + 1)
                nc.gpsimd.tensor_copy(cat_hi[:, KT:CT, rows], ctx_hi[:])
                nc.gpsimd.tensor_tensor(cat_lo[:, KT:CT, rows], ctx_norm[:], ctx_hi[:].bitcast(F32),
                                        ALU.subtract).then_inc(ctx_split, 1)

            last_place = nc.gpsimd.to_reg(B * ITEMS - 1)
            with pool.Fori(0, SCATTER_FROM) as i:
                copies(i)
            pool.wait_ge(mask_zeroed, 16 * ZERO_PARTS * ROW_TILES)
            with pool.Fori(0, SCATTER_BODIES) as i:
                nc.gpsimd.tensor_copy(where_body[:], where[:, bass.ds(i * SLOTS, SLOTS)]).then_inc(where_copied, 1)
                pool.wait_ge(where_copied, 1)
                for s in range(SLOTS):
                    nc.gpsimd.tensor_tensor(where_now[:, s:s + 1], where_body[:, s:s + 1], zero[:],
                                            ALU.add).then_inc(where_copied, 1)
                    pool.wait_ge(where_copied, 2 + s)
                    nc.gpsimd.indirect_dma_start(
                        out=mask_bias, out_offset=bass.IndirectOffsetOnAxis(ap=where_now[:, s:s + 1], axis=0),
                        in_=masked_const[:], in_offset=None,
                        bounds_check=last_place, oob_is_err=False).then_inc(scattered, 16)
                    pool.wait_ge(scattered, i * (16 * SLOTS) + 16 * (s + 1))
                copies(i + SCATTER_FROM)
                pool.sem_clear(where_copied)
            pool.sem_inc(mask_complete, 1)
            with pool.Fori(SCATTER_FROM + SCATTER_BODIES, BODIES - 1) as i:
                copies(i)
            copies(BODIES - 1, last_body=True)

            pool.wait_ge(scale_made, RT)
            for g in range(GROUPS):
                if g == 0:
                    pool.wait_ge(scaled_dve, 1)
                    pool.wait_ge(scaled_act, 1)
                else:
                    pool.wait_ge(item_used[0], CHUNKS + STORE_EVERY * g)
                for r in range(RT if g > 0 else 0):
                    p = probs[:, r].rearrange("p (c i) -> p c i", i=CHUNK)[:, g * GROUP:(g + 1) * GROUP]
                    scale = chunk_scale[:, 0, r, g * GROUP:(g + 1) * GROUP]
                    nc.gpsimd.tensor_tensor(p, p, scale.unsqueeze(2).to_broadcast([P, GROUP, CHUNK]),
                                            ALU.mult).then_inc(scaled_pool, 1)
                wait(pool, scaled_pool, RT * g)
                wait(pool, stored_a, 16 * g)
                cols = slice(g * GROUP * CHUNK, (g + 1) * GROUP * CHUNK)
                pool.dma_start(out_halves[0, :, :, cols], probs[:, :, cols]).then_inc(stored_a, 16)
            pool.wait_ge(stored_a, 16 * GROUPS)

        @block.scalar
        def _(act):
            for k in range(KT):
                act.dma_start(we_raw[:, k], we_l[:, k]).then_inc(we_loaded[k], 16)
            act.dma_start(ue_raw[:], ue_l).then_inc(ue_loaded, 16)
            act.dma_start(ve[:], ve_l).then_inc(ve_loaded, 16)
            act.wait_ge(ones_set, 1)
            nc.scalar.activation(ones[:], ones_f[:], ACT.Copy).then_inc(ones_set, 1)

            def split_x(i, u):
                act.wait_ge(x_loaded[u % SLOTS], (i + 1) * 16)
                wait(act, keys_made, (i * SLOTS + (u - 1)) * KT)
                for k in (slice(0, KT // 2), slice(KT // 2, KT)):
                    nc.scalar.activation(x_hi[u % 2][:, k], x[u % SLOTS][:, k], ACT.Copy).then_inc(x_hi_made, 1)

            def split_item(n, pc):
                act.wait_ge(item_loaded[pc], (n + 1) * 16)
                wait(act, item_used[pc], n)
                nc.scalar.activation(item_hi[:, pc], item[:, pc], ACT.Copy).then_inc(item_hi_made[pc], 1)

            def split_weighted(i, u):
                act.wait_ge(weighted_made, (i * SLOTS + u) * (KT - 1))
                wait(act, scores_made, i * SLOTS + (u - 2))
                nc.scalar.activation(weighted_hi[:, (u - 1) % 2], weighted[:, (u - 1) % 2],
                                     ACT.Copy).then_inc(weighted_hi_made, 1)

            def attention(i, u):
                act.wait_ge(neg_max_made, i * SLOTS + u)
                wait(act, ctx_made, (i * SLOTS + (u - 2)) * STEP_ROWS)
                if u == 1:
                    wait(act, denom_rec_made, i)
                for g in range(STEP_ROWS):
                    cols = slice(g * S, (g + 1) * S)
                    row = (u - 1) % SLOTS * STEP_ROWS + g
                    nc.scalar.activation(attn[:, (u - 1) % 2, cols], score_ps[:, (u - 1) % 2, cols], ACT.Exp,
                                         bias=neg_max[:, (u - 1) % 2, g:g + 1],
                                         accum_out=denom_now[:, row:row + 1]).then_inc(attn_made, 1)

            def tanh(i, u, m):
                act.wait_ge(keys_made, (i * SLOTS + u) * KT + (m + 1))
                if m > 0:
                    wait(act, weighted_made, (i * SLOTS + (u - 2)) * (KT - 1) + m)
                for g in range(STEP_ROWS):
                    cols = slice(g * S, (g + 1) * S)
                    row = u * STEP_ROWS + g
                    made = nc.scalar.activation(th[u % 2][:, m, cols], k_ps[:, m, cols], ACT.Tanh,
                                                bias=q_now[:, m, row:row + 1])
                made.then_inc(tanh_made, 1)

            def weigh_first(i, u):
                act.wait_ge(tanh_made, (i * SLOTS + u) * KT + 1)
                wait(act, weighted_lo_made, i * SLOTS + (u - 1))
                nc.scalar.activation(weighted[:, u % 2], th[u % 2][:, 0], ACT.Copy,
                                     scale=ve[:, 0:1]).then_inc(weighed_first, 1)

            def step(i, u, first=False, final=False):
                if not first:
                    split_weighted(i, u)
                if not final:
                    split_x(i + (u + 1) // SLOTS, (u + 1) % SLOTS)
                else:
                    split_item(0, 0)
                    split_item(0, 1)
                if u == 0:
                    act.wait_ge(q_staged, i + 1)
                tanh(i, u, 0)
                tanh(i, u, 1)
                weigh_first(i, u)
                if not first:
                    attention(i, u)
                for m in range(2, KT):
                    tanh(i, u, m)

            split_x(0, 0)
            act.wait_ge(ue_loaded, 16)
            for m in range(KT):
                nc.scalar.activation(ue_hi[:, m], ue_raw[:, m], ACT.Copy).then_inc(ue_hi_made, 1)
            act.wait_ge(ve_loaded, 16)
            for u in range(SLOTS):
                step(0, u, first=(u == 0))
                act.wait_ge(last_loaded[u], 16)
                nc.scalar.activation(cat_hi[:, u], last[:, u], ACT.Copy).then_inc(cat_hi_made, 1)
            with act.Fori(1, BODIES - 1) as i:
                for u in range(SLOTS):
                    step(i, u)
            for u in range(SLOTS):
                step(BODIES - 1, u, final=(u == SLOTS - 1))
            split_weighted(BODIES, 0)

            def load_mask(half, rt, c):
                act.dma_start(masks[:, rt], mask_rows[rows_of(half, rt), bass.ds(c * CHUNK, CHUNK)]) \
                   .then_inc(mask_loaded[rt], 16)

            def exponentiate(half, rt, c, next_mask=True):
                act.wait_ge(neg_made[rt], c + (half * CHUNKS + 1))
                nc.scalar.activation(probs[:, rt, bass.ds(c * CHUNK, CHUNK)], raw_logits[:, rt], ACT.Exp,
                                     bias=chunk_neg_max[:, half, rt, bass.ds(c, 1)],
                                     accum_out=chunk_sum[:, half, rt, bass.ds(c, 1)]).then_inc(exp_made[rt], 1)
                if next_mask:
                    load_mask(half, rt, c + 1)

            for pc in range(2, PIECES):
                split_item(0, pc)
            act.wait_ge(mask_complete, 1)
            for rt in range(RT):
                load_mask(0, rt, 0)
            attention(BODIES, 0)

            def chunk(half, c, last_of_half=False, last_of_all=False, stored=None):
                n = c + half * CHUNKS
                if not last_of_all:
                    for pc in range(PIECES - 1 if stored is None else PIECES):
                        split_item(n + 1, pc)
                if stored is not None:
                    act.wait_ge(stored_a, stored)
                exponentiate(half, 0, c, not last_of_half)
                if not last_of_all and stored is None:
                    split_item(n + 1, PIECES - 1)
                exponentiate(half, 1, c, not last_of_half)

            def factors(half):
                act.wait_ge(row_max_made, half + 1)
                for rt in range(RT):
                    nc.scalar.activation(chunk_factor[:, half, rt], chunk_neg_max[:, half, rt], ACT.Exp,
                                         scale=-1.0, bias=row_neg_max[:, half, rt:rt + 1]).then_inc(factor_made, 1)

            def scale_group(half, g):
                for c in range(g * GROUP, (g + 1) * GROUP):
                    p = probs[:, 1, c * CHUNK:(c + 1) * CHUNK]
                    scaled = nc.scalar.activation(p, p, ACT.Copy, scale=chunk_scale[:, half, 1, c:c + 1])
                scaled.then_inc(scaled_act, 1)

            with act.Fori(0, CHUNKS - 1) as c:
                chunk(0, c)
            chunk(0, CHUNKS - 1, last_of_half=True)
            for rt in range(RT):
                load_mask(1, rt, 0)
            factors(0)
            act.wait_ge(scale_made, RT)
            scale_group(0, 0)
            with act.Fori(0, GROUPS - 1) as g:
                for c in range(GROUP):
                    chunk(1, g * GROUP + c, stored=(g * 16 + 16 if c == 0 else None))
            for c in range(CHUNKS - GROUP, CHUNKS):
                chunk(1, c, last_of_half=(c == CHUNKS - 1), last_of_all=(c == CHUNKS - 1),
                      stored=(GROUPS * 16 if c == CHUNKS - GROUP else None))
            factors(1)
            act.wait_ge(scale_made, RT * HALVES)
            for g in range(GROUPS):
                scale_group(1, g)
                act.wait_ge(scaled_act, g + 2)
                cols = slice(g * GROUP * CHUNK, (g + 1) * GROUP * CHUNK)
                act.dma_start(out[rows_of(1, 1), cols], probs[:, 1, cols]).then_inc(stored_act, 16)
            act.wait_ge(stored_act, 16 * GROUPS)

        @block.vector
        def _(dve):
            def split_x(i, u):
                for n, k in enumerate((slice(0, KT // 2), slice(KT // 2, KT))):
                    dve.wait_ge(x_hi_made, i * (SLOTS * 2) + (u * 2 + n + 1))
                    nc.vector.tensor_tensor(x_lo[u % 2][:, k], x[u % SLOTS][:, k], x_hi[u % 2][:, k].bitcast(F32),
                                            ALU.subtract).then_inc(x_lo_made, 1)

            def split_weighted(i, u):
                dve.wait_ge(weighted_hi_made, i * SLOTS + u)
                nc.vector.tensor_tensor(weighted_lo[:, (u - 1) % 2], weighted[:, (u - 1) % 2],
                                        weighted_hi[:, (u - 1) % 2].bitcast(F32),
                                        ALU.subtract).then_inc(weighted_lo_made, 1)

            def weigh(i, u, m):
                dve.wait_ge(tanh_made, (i * SLOTS + u) * KT + (m + 1))
                w = weighted[:, u % 2]
                if m == 1:
                    dve.wait_ge(weighed_first, i * SLOTS + (u + 1))
                else:
                    dve.wait_ge(weighted_made, (i * SLOTS + u) * (KT - 1) + (m - 1))
                nc.vector.scalar_tensor_tensor(w, th[u % 2][:, m], ve[:, m:m + 1], w,
                                               ALU.mult, ALU.add).then_inc(weighted_made, 1)

            def maximum(i, u):
                dve.wait_ge(scores_made, i * SLOTS + u)
                s = score_ps[:, (u - 1) % 2, 0:COLS].rearrange("p (g s) -> p g s", g=STEP_ROWS)
                wait(dve, attn_made, (i * SLOTS + (u - 2)) * STEP_ROWS)
                nc.vector.tensor_reduce(neg_max[:, (u - 1) % 2], s, AX_X, ALU.max,
                                        negate=True).then_inc(neg_max_made, 1)

            def pool_memory(i, u, g):
                dve.wait_ge(attn_made, (i * SLOTS + (u - 1)) * STEP_ROWS + (g + 1))
                cols = slice(g * S, (g + 1) * S)
                row = (u - 1) % SLOTS * STEP_ROWS + g
                for k in range(KT):
                    xs = x[(u - 1) % SLOTS][:, k, cols]
                    made = nc.vector.tensor_tensor_reduce(xs, xs, attn[:, (u - 1) % 2, cols], 1.0, 0.0, ALU.mult,
                                                          ALU.add, ctx_now[:, k, row:row + 1])
                made.then_inc(ctx_made, 1)

            def split_item(n, pc):
                dve.wait_ge(item_hi_made[pc], n + 1)
                nc.vector.tensor_tensor(item_lo[:, pc], item[:, pc], item_hi[:, pc].bitcast(F32),
                                        ALU.subtract).then_inc(item_lo_made[pc], 1)

            def normalise(i):
                nc.vector.reciprocal(denom_rec[:], denom_now[:]).then_inc(denom_rec_made, 1)
                dve.wait_ge(denom_rec_made, i)
                dve.wait_ge(ctx_made, i * (SLOTS * STEP_ROWS))
                dve.wait_ge(ctx_split, i)
                nc.vector.tensor_tensor(ctx_norm[:], ctx_now[:],
                                        denom_rec[:].unsqueeze(1).to_broadcast([P, KT, BODY_ROWS]),
                                        ALU.mult).then_inc(ctx_normalised, 1)
                dve.wait_ge(ctx_normalised, i)
                nc.vector.tensor_copy(ctx_hi[:], ctx_norm[:]).then_inc(ctx_hi_made, 1)

            def step(i, u, first=False, final=False):
                if not first:
                    split_weighted(i, u)
                if not final:
                    split_x(i + (u + 1) // SLOTS, (u + 1) % SLOTS)
                else:
                    split_item(0, 0)
                    split_item(0, 1)
                if not first:
                    maximum(i, u)
                weigh(i, u, 1)
                if not first:
                    pool_memory(i, u, 0)
                weigh(i, u, 2)
                if not first:
                    pool_memory(i, u, 1)
                if u == 0 and not first:
                    normalise(i)
                weigh(i, u, 3)

            split_x(0, 0)
            dve.wait_ge(ue_loaded, 16)
            for m in range(KT):
                dve.wait_ge(ue_hi_made, m + 1)
                nc.vector.tensor_tensor(ue_lo[:, m], ue_raw[:, m], ue_hi[:, m].bitcast(F32),
                                        ALU.subtract).then_inc(ue_lo_made, 1)
            for m in range(KT):
                dve.wait_ge(q_made, m + 1)
                nc.vector.tensor_copy(q_t[:, m], k_ps[:, m]).then_inc(q_copied, 1)
            dve.wait_ge(ve_loaded, 16)
            for u in range(SLOTS):
                step(0, u, first=(u == 0))
                dve.wait_ge(cat_hi_made, u + 1)
                nc.vector.tensor_tensor(cat_lo[:, u], last[:, u], cat_hi[:, u].bitcast(F32),
                                        ALU.subtract).then_inc(cat_lo_made, 1)
            with dve.Fori(1, BODIES - 1) as i:
                for u in range(SLOTS):
                    step(i, u)
            for u in range(SLOTS):
                step(BODIES - 1, u, final=(u == SLOTS - 1))
            split_weighted(BODIES, 0)

            def take_logits(half, rt, c):
                n = c + half * CHUNKS
                dve.wait_ge(logits_made[rt], n + 1)
                dve.wait_ge(mask_loaded[rt], n * 16 + 16)
                wait(dve, exp_made[rt], n)
                nc.vector.tensor_tensor(raw_logits[:, rt], masks[:, rt], logit_ps[:, rt, 0:CHUNK],
                                        ALU.add).then_inc(logits_out[rt], 1)
                dve.wait_ge(logits_out[rt], n + 1)
                nc.vector.tensor_reduce(chunk_neg_max[:, half, rt, bass.ds(c, 1)], raw_logits[:, rt], AX_X,
                                        ALU.max, negate=True).then_inc(neg_made[rt], 1)

            for pc in range(2, PIECES):
                split_item(0, pc)
            maximum(BODIES, 0)
            for g in range(STEP_ROWS):
                pool_memory(BODIES, 0, g)
            normalise(BODIES)

            def chunk(half, c, last_of_all=False):
                n = c + half * CHUNKS
                if not last_of_all:
                    split_item(n + 1, 0)
                    split_item(n + 1, 1)
                take_logits(half, 0, c)
                if not last_of_all:
                    split_item(n + 1, 2)
                take_logits(half, 1, c)
                if not last_of_all:
                    split_item(n + 1, 3)

            def scales(half):
                for rt in range(RT):
                    dve.wait_ge(neg_made[rt], (half + 1) * CHUNKS)
                nc.vector.tensor_reduce(row_neg_max[:, half], chunk_neg_max[:, half], AX_X,
                                        ALU.min).then_inc(row_max_made, 1)
                dve.wait_ge(factor_made, RT * (half + 1))
                for rt in range(RT):
                    dve.wait_ge(exp_made[rt], (half + 1) * CHUNKS)
                    nc.vector.tensor_tensor_reduce(factor_times_sum[:, half, rt], chunk_factor[:, half, rt],
                                                   chunk_sum[:, half, rt], 1.0, 0.0, ALU.mult, ALU.add,
                                                   row_sum[:, half, rt:rt + 1]).then_inc(sum_made, 1)
                dve.wait_ge(sum_made, RT * (half + 1))
                nc.vector.reciprocal(row_rec[:, half], row_sum[:, half]).then_inc(rec_made, 1)
                dve.wait_ge(rec_made, half + 1)
                for rt in range(RT):
                    nc.vector.tensor_scalar(chunk_scale[:, half, rt], chunk_factor[:, half, rt],
                                            row_rec[:, half, rt:rt + 1], None, ALU.mult).then_inc(scale_made, 1)

            def scale_group(half, g):
                for c in range(g * GROUP, (g + 1) * GROUP):
                    p = probs[:, 0, c * CHUNK:(c + 1) * CHUNK]
                    scaled = nc.vector.tensor_scalar(p, p, chunk_scale[:, half, 0, c:c + 1], None, ALU.mult)
                scaled.then_inc(scaled_dve, 1)

            chunk(0, 0)
            with dve.Fori(1, CHUNKS) as c:
                chunk(0, c)
            scales(0)
            dve.wait_ge(scale_made, RT)
            scale_group(0, 0)
            with dve.Fori(0, CHUNKS - 1) as c:
                chunk(1, c)
            chunk(1, CHUNKS - 1, last_of_all=True)
            scales(1)
            dve.wait_ge(scale_made, RT * HALVES)
            for g in range(GROUPS):
                scale_group(1, g)

        @block.tensor
        def _(pe):
            for k in range(KT):
                pe.wait_ge(we_loaded[k], 16)
                pe.wait_ge(last_loaded[k], 16)
                for m in range(KT):
                    made = nc.tensor.matmul(k_ps[:, m, :], we_raw[:, k, m * P:(m + 1) * P], last[:, k],
                                            start=(k == 0), stop=(k == KT - 1))
                    if k == KT - 1:
                        made.then_inc(q_made, 1)

            def keys(i, u, m):
                if isinstance(i, int) and i == 0 and u == 0:
                    pe.wait_ge(q_copied, m + 1)
                wait(pe, tanh_made, (i * SLOTS + (u - 1)) * KT + (m + 1))
                hi, lo = x_hi[u % 2], x_lo[u % 2]
                for k in range(KT):
                    w = slice(m * P, (m + 1) * P)
                    for n, (weights, moving) in enumerate(((ue_hi, hi), (ue_hi, lo), (ue_lo, hi))):
                        made = nc.tensor.matmul(k_ps[:, m, 0:COLS], weights[:, k, w], moving[:, k],
                                                start=(k == 0 and n == 0), stop=(k == KT - 1 and n == 2))
                made.then_inc(keys_made, 1)

            def scores(i, u):
                pe.wait_ge(weighted_hi_made, i * SLOTS + u)
                pe.wait_ge(weighted_lo_made, i * SLOTS + u)
                wait(pe, attn_made, (i * SLOTS + (u - 2)) * STEP_ROWS)
                b = (u - 1) % 2
                nc.tensor.matmul(score_ps[:, b, 0:COLS], ones[:], weighted_hi[:, b], start=True, stop=False)
                nc.tensor.matmul(score_ps[:, b, 0:COLS], ones[:], weighted_lo[:, b], start=False,
                                 stop=True).then_inc(scores_made, 1)

            def step(i, u, first=False):
                pe.wait_ge(x_hi_made, i * (SLOTS * 2) + (u + 1) * 2)
                pe.wait_ge(x_lo_made, i * (SLOTS * 2) + (u + 1) * 2)
                keys(i, u, 0)
                keys(i, u, 1)
                if not first:
                    scores(i, u)
                keys(i, u, 2)
                keys(i, u, 3)

            pe.wait_ge(ones_set, 2)
            pe.wait_ge(ue_hi_made, KT)
            pe.wait_ge(ue_lo_made, KT)
            for u in range(SLOTS):
                step(0, u, first=(u == 0))
            with pe.Fori(1, BODIES) as i:
                for u in range(SLOTS):
                    step(i, u)

            def products(half, pieces, rt):
                for pc in pieces:
                    for k in range(PIECE):
                        tile = pc * PIECE + k
                        w = slice((half * RT + rt) * P, (half * RT + rt + 1) * P)
                        for a, (weights, moving) in enumerate(((cat_hi, item_hi), (cat_hi, item_lo),
                                                               (cat_lo, item_hi))):
                            made = nc.tensor.matmul(logit_ps[:, rt, 0:CHUNK], weights[:, tile, w], moving[:, pc, k],
                                                    start=(tile == 0 and a == 0), stop=(tile == CT - 1 and a == 2))
                    if rt == RT - 1:
                        made.then_inc(item_used[pc], 1)
                return made

            def chunk(half, c, first=False):
                n = c + half * CHUNKS
                for part in range(2):
                    pieces = range(part * PIECES // 2, (part + 1) * PIECES // 2)
                    if first and part == 0:
                        pe.wait_ge(cat_hi_made, KT)
                        pe.wait_ge(cat_lo_made, KT)
                    if first and part == 1:
                        scores(BODIES, 0)
                        pe.wait_ge(ctx_split, BODIES // HALVES + 1)
                    for pc in pieces:
                        pe.wait_ge(item_hi_made[pc], n + 1)
                        pe.wait_ge(item_lo_made[pc], n + 1)
                    for rt in range(RT):
                        if part == 0:
                            wait(pe, logits_out[rt], n)
                        made = products(half, pieces, rt)
                        if part == 1 and rt < RT - 1:
                            made.then_inc(logits_made[rt], 1)

            chunk(0, 0, first=True)
            with pe.Fori(1, CHUNKS) as c:
                chunk(0, c)
            pe.wait_ge(ctx_split, BODIES + 1)
            with pe.Fori(0, CHUNKS) as c:
                chunk(1, c)


def kernel(r_last_memory, r_all_memory, r_mask, L0_rec_item_matrix_transpose, L0_rec_We, L0_rec_Ue, L0_rec_Ve):
    import concourse.bacc as bacc
    from concourse.bass_utils import run_bass_kernel_spmd

    B, S, H = r_all_memory.shape
    ITEMS = L0_rec_item_matrix_transpose.shape[1]
    KT = H // P
    chunks = ITEMS // CHUNK

    def features_first(w):
        return np.ascontiguousarray(np.asarray(w).reshape(-1, KT, P).transpose(2, 1, 0))

    x = np.asarray(r_all_memory).reshape(B // STEP_ROWS, STEP_ROWS * S, KT, P).transpose(0, 3, 2, 1)
    items = np.asarray(L0_rec_item_matrix_transpose).reshape(2, H, chunks, CHUNK)[::-1]
    items = items.reshape(2 * KT // PIECE, PIECE, P, chunks, CHUNK).transpose(3, 0, 2, 1, 4)
    arrays = {
        "x_l": np.ascontiguousarray(x),
        "last_l": features_first(r_last_memory),
        "we_l": features_first(L0_rec_We),
        "ue_l": features_first(L0_rec_Ue),
        "ve_l": features_first(L0_rec_Ve)[:, :, 0],
        "items_l": np.ascontiguousarray(items),
        "hist": np.ascontiguousarray(np.asarray(r_mask)),
    }
    nc = bacc.Bacc("TRN2", target_bir_lowering=False, num_devices=1)
    args = {name: nc.dram_tensor(name, a.shape, mybir.dt.from_np(a.dtype), kind="ExternalInput").ap()
            for name, a in arrays.items()}
    out = nc.dram_tensor("probs_out", (B, ITEMS), F32, kind="ExternalOutput").ap()
    attention_rank(nc, out=out, **args)
    result = run_bass_kernel_spmd(nc, [arrays], core_ids=[0])
    return result.results[0]["probs_out"]
```
